# Optimizing a Trainium2 kernel written in Bass

```python
import numpy as np
import jax
import jax.numpy as jnp

def _softmax(x, axis=-1):
    return jax.nn.softmax(x, axis=axis)

def _gelu(x):
    return jax.nn.gelu(x, approximate=True)

def _silu(x):
    return jax.nn.silu(x)

def _sigmoid(x):
    return jax.nn.sigmoid(x)

def _layernorm(x, axis=-1, eps=1e-05):
    m = jnp.mean(x, axis=axis, keepdims=True)
    v = jnp.var(x, axis=axis, keepdims=True)
    return (x - m) / jnp.sqrt(v + eps)

def _scatter_add(tgt, idx, src, axis=0):
    return tgt.at[idx].add(src)

def _segment_sum(src, seg, n):
    return jax.ops.segment_sum(src, seg, n)
kernel_name = 'mk_dlrm_tower_d1_rec_r8_3b22b2'

def setup_inputs(seed: int=0):
    np.random.seed(seed)
    _w = jnp.asarray

    def _rec_inputs():
        import jax
        import jax.numpy as jnp
        _tk = jax.random.key(seed)
        dense_ctx = jax.random.normal(jax.random.fold_in(_tk, 190), (2048, 16), jnp.float32)
        ids = jnp.stack([jax.random.randint(jax.random.fold_in(_tk, 200 + f), (2048,), 0, v, jnp.int32) for f, v in enumerate([1000, 12500, 1250, 125000, 12500, 1000, 1000, 12500, 1250, 12500, 1250, 12500, 12500, 12500, 1250, 1000, 12500, 12500, 1000, 1000, 1000, 1000, 1000, 1000, 1000, 1000, 1000])], axis=1)
        tbl_0 = 0.05 * jax.random.normal(jax.random.fold_in(_tk, 500 + 0), (1000, 128), jnp.float32)
        tbl_1 = 0.05 * jax.random.normal(jax.random.fold_in(_tk, 500 + 1), (12500, 128), jnp.float32)
        tbl_2 = 0.05 * jax.random.normal(jax.random.fold_in(_tk, 500 + 2), (1250, 128), jnp.float32)
        tbl_3 = 0.05 * jax.random.normal(jax.random.fold_in(_tk, 500 + 3), (125000, 128), jnp.float32)
        tbl_4 = 0.05 * jax.random.normal(jax.random.fold_in(_tk, 500 + 4), (12500, 128), jnp.float32)
        tbl_5 = 0.05 * jax.random.normal(jax.random.fold_in(_tk, 500 + 5), (1000, 128), jnp.float32)
        tbl_6 = 0.05 * jax.random.normal(jax.random.fold_in(_tk, 500 + 6), (1000, 128), jnp.float32)
        tbl_7 = 0.05 * jax.random.normal(jax.random.fold_in(_tk, 500 + 7), (12500, 128), jnp.float32)
        tbl_8 = 0.05 * jax.random.normal(jax.random.fold_in(_tk, 500 + 8), (1250, 128), jnp.float32)
        tbl_9 = 0.05 * jax.random.normal(jax.random.fold_in(_tk, 500 + 9), (12500, 128), jnp.float32)
        tbl_10 = 0.05 * jax.random.normal(jax.random.fold_in(_tk, 500 + 10), (1250, 128), jnp.float32)
        tbl_11 = 0.05 * jax.random.normal(jax.random.fold_in(_tk, 500 + 11), (12500, 128), jnp.float32)
        tbl_12 = 0.05 * jax.random.normal(jax.random.fold_in(_tk, 500 + 12), (12500, 128), jnp.float32)
        tbl_13 = 0.05 * jax.random.normal(jax.random.fold_in(_tk, 500 + 13), (12500, 128), jnp.float32)
        tbl_14 = 0.05 * jax.random.normal(jax.random.fold_in(_tk, 500 + 14), (1250, 128), jnp.float32)
        tbl_15 = 0.05 * jax.random.normal(jax.random.fold_in(_tk, 500 + 15), (1000, 128), jnp.float32)
        tbl_16 = 0.05 * jax.random.normal(jax.random.fold_in(_tk, 500 + 16), (12500, 128), jnp.float32)
        tbl_17 = 0.05 * jax.random.normal(jax.random.fold_in(_tk, 500 + 17), (12500, 128), jnp.float32)
        tbl_18 = 0.05 * jax.random.normal(jax.random.fold_in(_tk, 500 + 18), (1000, 128), jnp.float32)
        tbl_19 = 0.05 * jax.random.normal(jax.random.fold_in(_tk, 500 + 19), (1000, 128), jnp.float32)
        tbl_20 = 0.05 * jax.random.normal(jax.random.fold_in(_tk, 500 + 20), (1000, 128), jnp.float32)
        tbl_21 = 0.05 * jax.random.normal(jax.random.fold_in(_tk, 500 + 21), (1000, 128), jnp.float32)
        tbl_22 = 0.05 * jax.random.normal(jax.random.fold_in(_tk, 500 + 22), (1000, 128), jnp.float32)
        tbl_23 = 0.05 * jax.random.normal(jax.random.fold_in(_tk, 500 + 23), (1000, 128), jnp.float32)
        tbl_24 = 0.05 * jax.random.normal(jax.random.fold_in(_tk, 500 + 24), (1000, 128), jnp.float32)
        tbl_25 = 0.05 * jax.random.normal(jax.random.fold_in(_tk, 500 + 25), (1000, 128), jnp.float32)
        tbl_26 = 0.05 * jax.random.normal(jax.random.fold_in(_tk, 500 + 26), (1000, 128), jnp.float32)
        _rk = jax.random.fold_in(_tk, 7)
        W_top1 = 0.0161733 * jax.random.normal(jax.random.fold_in(_tk, 801), (3823, 512), jnp.float32)
        W_top2 = 0.0441942 * jax.random.normal(jax.random.fold_in(_tk, 802), (512, 256), jnp.float32)
        W_top3 = 0.0625 * jax.random.normal(jax.random.fold_in(_tk, 803), (256, 1), jnp.float32)
        b_top1 = jnp.zeros((512,), jnp.float32)
        b_top2 = jnp.zeros((256,), jnp.float32)
        return (dense_ctx, ids, tbl_0, tbl_1, tbl_2, tbl_3, tbl_4, tbl_5, tbl_6, tbl_7, tbl_8, tbl_9, tbl_10, tbl_11, tbl_12, tbl_13, tbl_14, tbl_15, tbl_16, tbl_17, tbl_18, tbl_19, tbl_20, tbl_21, tbl_22, tbl_23, tbl_24, tbl_25, tbl_26, W_top1, b_top1, W_top2, b_top2, W_top3)
    dense_ctx, ids, tbl_0, tbl_1, tbl_2, tbl_3, tbl_4, tbl_5, tbl_6, tbl_7, tbl_8, tbl_9, tbl_10, tbl_11, tbl_12, tbl_13, tbl_14, tbl_15, tbl_16, tbl_17, tbl_18, tbl_19, tbl_20, tbl_21, tbl_22, tbl_23, tbl_24, tbl_25, tbl_26, W_top1, b_top1, W_top2, b_top2, W_top3 = _rec_inputs()

    def _L0_rec_setup():
        import jax, jax.numpy as jnp
        import numpy as np
        NUM_FEATURES = 27
        FEATURE_DIM = 128
        BATCH = 2048
        _TRIU_I, _TRIU_J = np.triu_indices(NUM_FEATURES, k=1)
        key = jax.random.key(seed)
        embeddings = jax.random.normal(key, (BATCH, NUM_FEATURES, FEATURE_DIM), dtype=jnp.float32)
        return {'embeddings': embeddings}
    _L0_rec_all = _L0_rec_setup()
    _L0_rec_in = {k: v for k, v in _L0_rec_all.items() if k in ()}
    del _L0_rec_all
    return {'dense_ctx': dense_ctx, 'ids': ids, 'tbl_0': tbl_0, 'tbl_1': tbl_1, 'tbl_2': tbl_2, 'tbl_3': tbl_3, 'tbl_4': tbl_4, 'tbl_5': tbl_5, 'tbl_6': tbl_6, 'tbl_7': tbl_7, 'tbl_8': tbl_8, 'tbl_9': tbl_9, 'tbl_10': tbl_10, 'tbl_11': tbl_11, 'tbl_12': tbl_12, 'tbl_13': tbl_13, 'tbl_14': tbl_14, 'tbl_15': tbl_15, 'tbl_16': tbl_16, 'tbl_17': tbl_17, 'tbl_18': tbl_18, 'tbl_19': tbl_19, 'tbl_20': tbl_20, 'tbl_21': tbl_21, 'tbl_22': tbl_22, 'tbl_23': tbl_23, 'tbl_24': tbl_24, 'tbl_25': tbl_25, 'tbl_26': tbl_26, 'W_top1': W_top1, 'b_top1': b_top1, 'W_top2': W_top2, 'b_top2': b_top2, 'W_top3': W_top3}

def reference(dense_ctx, ids, tbl_0, tbl_1, tbl_2, tbl_3, tbl_4, tbl_5, tbl_6, tbl_7, tbl_8, tbl_9, tbl_10, tbl_11, tbl_12, tbl_13, tbl_14, tbl_15, tbl_16, tbl_17, tbl_18, tbl_19, tbl_20, tbl_21, tbl_22, tbl_23, tbl_24, tbl_25, tbl_26, W_top1, b_top1, W_top2, b_top2, W_top3):
    import jax
    import jax.numpy as jnp

    def _L0_rec_ref(embeddings):
        import jax, jax.numpy as jnp
        import numpy as np
        NUM_FEATURES = 27
        FEATURE_DIM = 128
        BATCH = 2048
        _TRIU_I, _TRIU_J = np.triu_indices(NUM_FEATURES, k=1)
        B = embeddings.shape[0]
        interactions = jnp.einsum('bfd,bgd->bfg', embeddings, embeddings)
        flat_interactions = interactions[:, _TRIU_I, _TRIU_J]
        flat_embeddings = embeddings.reshape(B, -1)
        return jnp.concatenate([flat_embeddings, flat_interactions], axis=1)
    e = jnp.stack([tbl_0[ids[:, 0]], tbl_1[ids[:, 1]], tbl_2[ids[:, 2]], tbl_3[ids[:, 3]], tbl_4[ids[:, 4]], tbl_5[ids[:, 5]], tbl_6[ids[:, 6]], tbl_7[ids[:, 7]], tbl_8[ids[:, 8]], tbl_9[ids[:, 9]], tbl_10[ids[:, 10]], tbl_11[ids[:, 11]], tbl_12[ids[:, 12]], tbl_13[ids[:, 13]], tbl_14[ids[:, 14]], tbl_15[ids[:, 15]], tbl_16[ids[:, 16]], tbl_17[ids[:, 17]], tbl_18[ids[:, 18]], tbl_19[ids[:, 19]], tbl_20[ids[:, 20]], tbl_21[ids[:, 21]], tbl_22[ids[:, 22]], tbl_23[ids[:, 23]], tbl_24[ids[:, 24]], tbl_25[ids[:, 25]], tbl_26[ids[:, 26]]], axis=1)
    z = _L0_rec_ref(e)
    z = z.reshape(z.shape[0], -1)
    h = jnp.concatenate([z, dense_ctx], axis=1)
    h = jnp.maximum(h @ W_top1 + b_top1, 0.0)
    h = jnp.maximum(h @ W_top2 + b_top2, 0.0)
    y = h @ W_top3
    return y

_drawn_inputs = setup_inputs


def setup_inputs(seed=0):
    import zlib

    import numpy as np

    out = dict(_drawn_inputs(seed))
    spreads = {'b_top1': (0.0, 0.1), 'b_top2': (0.0, 0.1)}
    factors = {}
    for name, (base, spread) in spreads.items():
        noise = np.random.default_rng([zlib.crc32(name.encode()), seed]).standard_normal(out[name].shape)
        drawn = base * np.exp(spread * noise) if base else spread * noise
        out[name] = jnp.asarray(drawn.astype(out[name].dtype))
    for name, factor in factors.items():
        out[name] = (out[name] * factor).astype(out[name].dtype)
    return out
```

```python
import concourse.bass as bass
from concourse import mybir
from contextlib import ExitStack


def dlrm_tower_kernel(nc, dense_ctx, ids, tables, w_top1, b_top1, w_top2, b_top2, w_top3, out):
    fp32 = mybir.dt.float32
    fp32r = mybir.dt.float32r
    i32 = mybir.dt.int32
    ALU = mybir.AluOpType
    ACT = mybir.ActivationFunctionType

    P = 128
    BATCH, NF = ids.shape
    D = tables[0].shape[1]
    NCTX = dense_ctx.shape[1]
    K1, H1 = w_top1.shape
    H2 = w_top2.shape[1]
    TILES = BATCH // P
    NPAIR = NF * (NF - 1) // 2
    NCOL = NPAIR + NCTX
    assert D == P and K1 == NF * D + NCOL and TILES % 2 == 0 and H1 == 512

    GF = 4
    GROUPS = [list(range(f, min(f + GF, NF))) for f in range(0, NF, GF)]
    NG = len(GROUPS)
    assert NG % 2 == 1
    COL_CHUNKS = [(c, min(P, NCOL - c)) for c in range(0, NCOL, P)]
    FULL = NCOL // P
    W1_CHUNKS = NF + len(COL_CHUNKS)
    K2 = H1 // P
    PER = H1 // H2
    W_CHUNKS = W1_CHUNKS + K2 // PER
    STAGES = 6

    Q = 32
    R = NF - 1
    HALF = Q // 2

    ctx = ExitStack()
    with ctx:
        def sb(name, shape, dt=fp32):
            return ctx.enter_context(nc.sbuf_tensor(name, shape, dt))

        def ps(name, shape):
            return ctx.enter_context(nc.psum_tensor(name, shape, fp32))

        def sem(name):
            return ctx.enter_context(nc.semaphore(name))

        w_hi = sb("w_hi", [P, W_CHUNKS, H1], fp32r)
        w_lo = sb("w_lo", [P, W_CHUNKS, H1], fp32r)
        emb = sb("emb", [P, NF * D])
        emb_t = sb("emb_t", [P, 2, NF * P])
        emb_hi = sb("emb_hi", [P, 2, GF * P], fp32r)
        emb_lo = sb("emb_lo", [P, 2, GF * P], fp32r)
        idx = sb("idx", [P, 2, NF], i32)
        ident = sb("ident", [P, P])
        gram = sb("gram", [P, R, Q])
        cols = sb("cols", [P, 2, NCOL])
        cols_hi = sb("cols_hi", [P, len(COL_CHUNKS) * P], fp32r)
        cols_lo = sb("cols_lo", [P, len(COL_CHUNKS) * P], fp32r)
        h1 = sb("h1", [P, H1])
        h1_t = sb("h1_t", [P, H1])
        h1_hi = sb("h1_hi", [P, H1], fp32r)
        h1_lo = sb("h1_lo", [P, H1], fp32r)
        h2 = sb("h2", [P, H2])
        h2_w = sb("h2_w", [P, H2])
        y = sb("y", [P, TILES])
        b1_rows = sb("b1_rows", [P, H1])
        b2_rows = sb("b2_rows", [P, H2])
        w3_rows = sb("w3_rows", [P, H2])
        stage = emb_t[:, 1, 0:STAGES * H1].rearrange("p (s n) -> p s n", s=STAGES)

        ps_t = ps("ps_t", [P, 2, GF * P])
        ps_acc = ps("ps_acc", [P, 2, H1])
        ps_gram = ps("ps_gram", [P, 2, 512])
        ps_late = ps("ps_late", [P, 512])
        ps_h2 = ps("ps_h2", [P, 512])

        s_ids = [sem(f"s_ids{p}") for p in range(2)]
        s_ctx = [sem(f"s_ctx{p}") for p in range(2)]
        s_const = sem("s_const")
        s_w_raw = [sem(f"s_w_raw{s}") for s in range(STAGES)]
        s_gather = [sem(f"s_gather{g}") for g in range(NG)]
        s_started = sem("s_started")
        s_zero = sem("s_zero")
        s_ident = sem("s_ident")
        s_gram_clear = sem("s_gram_clear")
        s_w_hi = sem("s_w_hi")
        s_w_lo = sem("s_w_lo")
        s_emb_t = sem("s_emb_t")
        s_emb_x = sem("s_emb_x")
        s_emb_lo = sem("s_emb_lo")
        s_emb_mm = sem("s_emb_mm")
        s_gram = sem("s_gram")
        s_gram_out = sem("s_gram_out")
        s_cols = sem("s_cols")
        s_cols_t = sem("s_cols_t")
        s_cols_hi = sem("s_cols_hi")
        s_cols_lo = sem("s_cols_lo")
        s_acc = sem("s_acc")
        s_h1 = sem("s_h1")
        s_h1_t = sem("s_h1_t")
        s_h1_last = sem("s_h1_last")
        s_h1_hi = sem("s_h1_hi")
        s_h1_lo = sem("s_h1_lo")
        s_l2 = sem("s_l2")
        s_h2 = sem("s_h2")
        s_y = sem("s_y")
        s_stored = sem("s_stored")

        LAST = (TILES - 1, TILES // 2 - 1, 1)

        def over_tiles(eng, tile):
            tile((0, 0, 0), None)
            tile((1, 0, 1), (0, 0, 0))
            with eng.Fori(1, TILES // 2) as i:
                tile((2 * i, i, 0), (2 * i - 1, i - 1, 1))
                tile((2 * i + 1, i, 1), (2 * i, i, 0))

        def is_first(t, n=1):
            return isinstance(t, int) and t < n

        block = ctx.enter_context(nc.Block())

        @block.sync
        def _(sp):
            def load_ids(t, p):
                sp.dma_start(idx[:, p, :], ids[bass.ds(t * P, P), :]).then_inc(s_ids[p], 16)

            def load_ctx(t, p):
                sp.dma_start(cols[:, p, NPAIR:NCOL],
                             dense_ctx[bass.ds(t * P, P), :]).then_inc(s_ctx[p], 16)

            def load_weights(c):
                if c >= STAGES:
                    sp.wait_ge(s_w_lo, c - STAGES + 1)
                s = c % STAGES
                if c < W1_CHUNKS:
                    rows = min(P, K1 - c * P)
                    sp.dma_start(stage[0:rows, s, :],
                                 w_top1[c * P:c * P + rows, :]).then_inc(s_w_raw[s], 16)
                else:
                    k = (c - W1_CHUNKS) * PER
                    sp.dma_start(stage[:, s, :].rearrange("p (k n) -> p k n", k=PER),
                                 w_top2[k * P:(k + PER) * P, :].rearrange("(k p) n -> p k n", p=P)
                                 ).then_inc(s_w_raw[s], 16)

            def store(t):
                sp.wait_ge(s_y, t + 1)
                sp.dma_start(out[bass.ds(t * P, P), :], y[:, bass.ds(t, 1)]).then_inc(s_stored, 16)

            load_ids(0, 0)
            load_weights(0)
            load_ids(1, 1)
            for c in range(1, W_CHUNKS):
                load_weights(c)

            def tile(t, p):
                sp.wait_ge(s_emb_t, NG * t)
                load_ids(t + 1, 1 - p)
                sp.wait_ge(s_cols_t, t)
                load_ctx(t + 1, 1 - p)
                store(t - 1)

            with sp.Fori(0, TILES // 2 - 1) as i:
                tile(2 * i + 1, 1)
                tile(2 * i + 2, 0)
            store(TILES - 2)
            store(TILES - 1)
            sp.wait_ge(s_stored, 16 * TILES)

        @block.gpsimd
        def _(pool):
            pool.memset(ident[:, :], 0.0).then_inc(s_zero, 1)
            pool.wait_ge(s_zero, 1)
            pool.affine_select(out=ident[:, :], in_=ident[:, :], compare_op=ALU.not_equal, fill=1.0,
                               base=0, pattern=[[-1, P]], channel_multiplier=1).then_inc(s_ident, 1)

            def tile(now, before):
                t, u, p = now
                pool.wait_ge(s_ids[p], 16 * u + 16)
                for g, group in enumerate(GROUPS):
                    if not is_first(t):
                        pool.wait_ge(s_emb_t, NG * t - NG + g + 1)
                    pool.sem_inc(s_started, 1)
                    for f in group:
                        pool.indirect_dma_start(
                            out=emb[:, f * D:(f + 1) * D], out_offset=None, in_=tables[f],
                            in_offset=bass.IndirectOffsetOnAxis(ap=idx[:, p, f:f + 1], axis=0)
                        ).then_inc(s_gather[g], 16)

            over_tiles(pool, tile)

        @block.tensor
        def _(pe):
            def transpose_group(t, p, g):
                slot = (p + g) % 2
                group = GROUPS[g]
                pe.wait_ge(s_gather[g], (t + 1) * (16 * len(group)))
                if not (is_first(t) and g < 2):
                    pe.wait_ge(s_emb_lo, NG * t + g - 1)
                for n, f in enumerate(group):
                    last = pe.transpose(ps_t[:, slot, n * P:(n + 1) * P],
                                        emb[:, f * D:(f + 1) * D], ident[:, :])
                last.then_inc(s_emb_t, 1)

            def split_product(acc, x_hi, x_lo, c, lo, hi, start, stop):
                rows = x_hi.shape[0]
                pe.matmul(acc, x_hi, w_hi[0:rows, c, lo:hi], start=start, stop=False)
                pe.matmul(acc, x_hi, w_lo[0:rows, c, lo:hi], start=False, stop=False)
                return pe.matmul(acc, x_lo, w_hi[0:rows, c, lo:hi], start=False, stop=stop)

            def multiply_group(t, p, g):
                slot = (p + g) % 2
                if g == 0 and not is_first(t, 2):
                    pe.wait_ge(s_h1, t - 1)
                pe.wait_ge(s_emb_lo, NG * t + g + 1)
                if is_first(t):
                    pe.wait_ge(s_w_lo, GROUPS[g][-1] + 1)
                for n, f in enumerate(GROUPS[g]):
                    last = split_product(ps_acc[:, p, :], emb_hi[:, slot, n * P:(n + 1) * P],
                                         emb_lo[:, slot, n * P:(n + 1) * P], f, 0, H1,
                                         start=(f == 0), stop=False)
                last.then_inc(s_emb_mm, 1)

            def gram_matrices(t, p, half):
                if half == 0:
                    pe.wait_ge(s_emb_x, NG * t + NG)
                    if is_first(t):
                        pe.wait_ge(s_gram_clear, 1)
                    else:
                        pe.wait_ge(s_gram_out, t)
                for q in range(half * HALF, (half + 1) * HALF):
                    for j in range(P // Q):
                        sample = emb_t[:, p, j * Q + q:NF * P:P]
                        last = pe.matmul(
                            ps_gram[j * Q:j * Q + R, q // HALF, (q % HALF) * R:(q % HALF + 1) * R],
                            sample[:, 0:R], sample[:, 1:NF], start=True, stop=True,
                            tile_position=(0, j * Q))
                if half == 1:
                    last.then_inc(s_gram, 1)

            def transpose_columns(t, u, p):
                pe.wait_ge(s_cols, t + 1)
                pe.wait_ge(s_ctx[p], 16 * u + 16)
                for n, (c, k) in enumerate(COL_CHUNKS):
                    last = pe.transpose(ps_late[0:k, n * P:(n + 1) * P], cols[:, p, c:c + k],
                                        ident[:, :])
                last.then_inc(s_cols_t, 1)

            def multiply_columns(t, p):
                pe.wait_ge(s_cols_hi, t + 1)
                pe.wait_ge(s_cols_lo, t + 1)
                for n, (c, k) in enumerate(COL_CHUNKS):
                    last = split_product(ps_acc[:, p, :], cols_hi[0:k, n * P:(n + 1) * P],
                                         cols_lo[0:k, n * P:(n + 1) * P], NF + n, 0, H1,
                                         start=False, stop=(n == len(COL_CHUNKS) - 1))
                last.then_inc(s_acc, 1)

            def transpose_h1(t):
                pe.wait_ge(s_h1, t + 1)
                for k in range(K2):
                    last = pe.transpose(ps_late[:, k * P:(k + 1) * P], h1[:, k * P:(k + 1) * P],
                                        ident[:, :])
                last.then_inc(s_h1_last, 1)

            def layer_2(t):
                pe.wait_ge(s_h1_hi, t + 1)
                pe.wait_ge(s_h1_lo, t + 1)
                if not is_first(t):
                    pe.wait_ge(s_h2, t)
                for k in range(K2):
                    last = split_product(ps_h2[:, 0:H2], h1_hi[:, k * P:(k + 1) * P],
                                         h1_lo[:, k * P:(k + 1) * P], W1_CHUNKS + k // PER,
                                         (k % PER) * H2, (k % PER + 1) * H2,
                                         start=(k == 0), stop=(k == K2 - 1))
                last.then_inc(s_l2, 1)

            def finish_tile(now):
                t, u, p = now
                gram_matrices(t, p, 1)
                multiply_group(t, p, NG - 1)

            def tile(now, before):
                t, u, p = now
                late = before is not None
                if not late:
                    transpose_group(t, p, 0)
                    for g in range(NG - 1):
                        transpose_group(t, p, g + 1)
                        multiply_group(t, p, g)
                    gram_matrices(t, p, 0)
                    pe.wait_ge(s_w_lo, W_CHUNKS)
                    return
                transpose_group(t, p, 0)
                finish_tile(before)
                transpose_group(t, p, 1)
                multiply_group(t, p, 0)
                transpose_group(t, p, 2)
                multiply_group(t, p, 1)
                transpose_columns(*before)
                transpose_group(t, p, 3)
                multiply_group(t, p, 2)
                multiply_columns(before[0], before[2])
                transpose_group(t, p, 4)
                multiply_group(t, p, 3)
                transpose_group(t, p, 5)
                multiply_group(t, p, 4)
                transpose_group(t, p, 6)
                multiply_group(t, p, 5)
                gram_matrices(t, p, 0)
                layer_2(before[0])

            pe.wait_ge(s_ident, 1)
            over_tiles(pe, tile)
            finish_tile(LAST)
            transpose_columns(*LAST)
            multiply_columns(LAST[0], LAST[2])
            transpose_h1(LAST[0])
            layer_2(LAST[0])

        @block.scalar
        def _(act):
            def split_weights(c):
                rows = min(P, K1 - c * P) if c < W1_CHUNKS else P
                act.wait_ge(s_w_raw[c % STAGES], 16 * (c // STAGES + 1))
                act.activation(w_hi[0:rows, c, :], stage[0:rows, c % STAGES, :],
                               ACT.Copy).then_inc(s_w_hi, 1)

            def copy_group(t, p, g):
                slot = (p + g) % 2
                f, n = GROUPS[g][0], len(GROUPS[g]) * P
                act.wait_ge(s_emb_t, NG * t + g + 1)
                if not (is_first(t) and g < 2):
                    act.wait_ge(s_emb_mm, NG * t + g - 1)
                act.activation(emb_hi[:, slot, 0:n], ps_t[:, slot, 0:n], ACT.Copy)
                act.activation(emb_t[:, p, f * P:f * P + n], ps_t[:, slot, 0:n],
                               ACT.Copy).then_inc(s_emb_x, 1)

            def split_columns(t):
                act.wait_ge(s_cols_t, t + 1)
                if not is_first(t):
                    act.wait_ge(s_acc, t)
                act.activation(cols_hi[:, 0:FULL * P], ps_late[:, 0:FULL * P], ACT.Copy)
                k = NCOL - FULL * P
                act.activation(cols_hi[0:k, FULL * P:(FULL + 1) * P],
                               ps_late[0:k, FULL * P:(FULL + 1) * P],
                               ACT.Copy).then_inc(s_cols_hi, 1)

            def split_h1(t, h1_turned, turned, count):
                act.wait_ge(turned, count)
                if not is_first(t):
                    act.wait_ge(s_l2, t)
                act.activation(h1_hi[:, :], h1_turned[:, :], ACT.Relu).then_inc(s_h1_hi, 1)

            act.dma_start(cols[:, 0, NPAIR:NCOL], dense_ctx[0:P, :]).then_inc(s_ctx[0], 16)
            act.dma_start(cols[:, 1, NPAIR:NCOL], dense_ctx[P:2 * P, :]).then_inc(s_ctx[1], 16)
            act.dma_start(b1_rows[:, :], b_top1.partition_broadcast(P)).then_inc(s_const, 16)
            act.dma_start(b2_rows[:, :], b_top2.partition_broadcast(P)).then_inc(s_const, 16)
            act.dma_start(w3_rows[:, :],
                          w_top3.rearrange("k o -> (k o)").partition_broadcast(P)
                          ).then_inc(s_const, 16)

            def tile(now, before):
                t, u, p = now
                if before is None:
                    for g, group in enumerate(GROUPS):
                        for c in group:
                            split_weights(c)
                        copy_group(t, p, g)
                    for c in range(NF, W_CHUNKS):
                        split_weights(c)
                    act.wait_ge(s_w_lo, W_CHUNKS)
                    return
                if not is_first(t, 2):
                    act.wait_ge(s_gram, t - 1)
                for g in range(NG):
                    copy_group(t, p, g)
                    if g == 2:
                        split_columns(before[0])
                split_h1(before[0], h1_t, s_h1_t, before[0] + 1)

            over_tiles(act, tile)
            split_columns(TILES - 1)
            split_h1(TILES - 1, ps_late, s_h1_last, 1)

        @block.vector
        def _(dve):
            def split_weights(c):
                rows = min(P, K1 - c * P) if c < W1_CHUNKS else P
                dve.wait_ge(s_w_hi, c + 1)
                dve.tensor_tensor(w_lo[0:rows, c, :], stage[0:rows, c % STAGES, :],
                                  w_hi[0:rows, c, :].bitcast(fp32),
                                  ALU.subtract).then_inc(s_w_lo, 1)

            def split_group(t, p, g):
                slot = (p + g) % 2
                n = len(GROUPS[g]) * P
                dve.wait_ge(s_emb_x, NG * t + g + 1)
                dve.tensor_tensor(emb_lo[:, slot, 0:n], ps_t[:, slot, 0:n],
                                  emb_hi[:, slot, 0:n].bitcast(fp32),
                                  ALU.subtract).then_inc(s_emb_lo, 1)

            def move_gram(t):
                dve.wait_ge(s_gram, t + 1)
                dve.transpose(gram[:, :, :].rearrange("p g f -> p (g f)"),
                              ps_gram[:, :, 0:HALF * R].rearrange("p h (q g) -> p g h q", g=R)
                              ).then_inc(s_gram_out, 1)

            def pack_pairs(t, p, f_from, f_to):
                if f_from == 0:
                    dve.wait_ge(s_gram_out, t + 1)
                    if not is_first(t):
                        dve.wait_ge(s_cols_t, t)
                for f in range(f_from, f_to):
                    c = f * NF - f * (f + 1) // 2
                    last = dve.tensor_copy(cols[:, p, c:c + R - f], gram[:, f:R, f])
                if f_to == R:
                    last.then_inc(s_cols, 1)

            def split_columns(t):
                dve.wait_ge(s_cols_hi, t + 1)
                dve.tensor_tensor(cols_lo[:, 0:FULL * P], ps_late[:, 0:FULL * P],
                                  cols_hi[:, 0:FULL * P].bitcast(fp32), ALU.subtract)
                k = NCOL - FULL * P
                last = slice(FULL * P, (FULL + 1) * P)
                dve.tensor_tensor(cols_lo[0:k, last], ps_late[0:k, last],
                                  cols_hi[0:k, last].bitcast(fp32),
                                  ALU.subtract).then_inc(s_cols_lo, 1)

            def bias_h1(t, p):
                dve.wait_ge(s_acc, t + 1)
                dve.tensor_tensor(h1[:, :], ps_acc[:, p, :], b1_rows[:, :],
                                  ALU.add).then_inc(s_h1, 1)

            def transpose_h1(t, i):
                if i == 0:
                    dve.wait_ge(s_h1, t + 1)
                rows = h1[:, :].rearrange("p (k c) -> p k c", c=P)
                turned = h1_t[:, :].rearrange("p (k b) -> p k b", b=P)
                for j in range(P // Q):
                    last = dve.transpose(turned[j * Q:(j + 1) * Q, :, i * Q:(i + 1) * Q],
                                         rows[i * Q:(i + 1) * Q, :, j * Q:(j + 1) * Q])
                if i == P // Q - 1:
                    last.then_inc(s_h1_t, 1)

            def split_h1(t, h1_turned):
                dve.wait_ge(s_h1_hi, t + 1)
                dve.scalar_tensor_tensor(out=h1_lo[:, :], in0=h1_turned[:, :], scalar=0.0,
                                         in1=h1_hi[:, :].bitcast(fp32), op0=ALU.max,
                                         op1=ALU.subtract).then_inc(s_h1_lo, 1)

            def layer_3(t):
                dve.wait_ge(s_l2, t + 1)
                dve.tensor_tensor(h2[:, :], ps_h2[:, 0:H2], b2_rows[:, :],
                                  ALU.add).then_inc(s_h2, 1)
                dve.wait_ge(s_h2, t + 1)
                dve.scalar_tensor_tensor(out=h2_w[:, :], in0=h2[:, :], scalar=0.0,
                                         in1=w3_rows[:, :], op0=ALU.max, op1=ALU.mult,
                                         accum_out=y[:, bass.ds(t, 1)]).then_inc(s_y, 1)

            def tile(now, before):
                t, u, p = now
                if before is None:
                    for g, group in enumerate(GROUPS):
                        for c in group:
                            split_weights(c)
                        split_group(t, p, g)
                    for c in range(NF, W_CHUNKS):
                        split_weights(c)
                    dve.wait_ge(s_const, 48)
                    return
                split_group(t, p, 0)
                move_gram(before[0])
                pack_pairs(before[0], before[2], 0, 12)
                split_group(t, p, 1)
                pack_pairs(before[0], before[2], 12, R)
                split_group(t, p, 2)
                split_columns(before[0])
                split_group(t, p, 3)
                bias_h1(before[0], before[2])
                transpose_h1(before[0], 0)
                split_group(t, p, 4)
                transpose_h1(before[0], 1)
                transpose_h1(before[0], 2)
                split_group(t, p, 5)
                transpose_h1(before[0], 3)
                split_group(t, p, 6)
                split_h1(before[0], h1_t)
                layer_3(before[0])

            dve.memset(ps_gram[:, :, :], 0.0).then_inc(s_gram_clear, 1)
            over_tiles(dve, tile)
            t, u, p = LAST
            move_gram(t)
            pack_pairs(t, p, 0, R)
            split_columns(t)
            bias_h1(t, p)
            split_h1(t, ps_late)
            layer_3(t)


N_TABLES = 27
_INS = (["dense_ctx", "ids"] + [f"tbl_{i}" for i in range(N_TABLES)]
        + ["W_top1", "b_top1", "W_top2", "b_top2", "W_top3"])


def kernel(**inputs):
    import numpy as np
    import concourse.bacc as bacc
    from concourse.bass_utils import run_bass_kernel_spmd

    nc = bacc.Bacc("TRN2", target_bir_lowering=False, num_devices=1)
    arrays, aps = {}, {}
    for name in _INS:
        a = np.ascontiguousarray(inputs[name])
        arrays[f"in_{name}"] = a
        aps[name] = nc.dram_tensor(f"in_{name}", a.shape, mybir.dt.from_np(a.dtype),
                                   kind="ExternalInput").ap()
    batch = inputs["ids"].shape[0]
    out = nc.dram_tensor("out", (batch, 1), mybir.dt.float32, kind="ExternalOutput").ap()
    dlrm_tower_kernel(nc, aps["dense_ctx"], aps["ids"], [aps[f"tbl_{i}"] for i in range(N_TABLES)],
                      aps["W_top1"], aps["b_top1"], aps["W_top2"], aps["b_top2"], aps["W_top3"], out)
    r = run_bass_kernel_spmd(nc, [arrays], core_ids=[0])
    return r.results[0]["out"]
```

```python
import concourse.bass as bass
from concourse import mybir
from contextlib import ExitStack


def dlrm_tower_kernel(nc, dense_ctx, ids, tables, w_top1, b_top1, w_top2, b_top2, w_top3, out):
    fp32 = mybir.dt.float32
    fp32r = mybir.dt.float32r
    i32 = mybir.dt.int32
    ALU = mybir.AluOpType
    ACT = mybir.ActivationFunctionType

    P = 128
    BATCH, NF = ids.shape
    D = tables[0].shape[1]
    NCTX = dense_ctx.shape[1]
    K1, H1 = w_top1.shape
    H2 = w_top2.shape[1]
    TILES = BATCH // P
    NPAIR = NF * (NF - 1) // 2
    NCOL = NPAIR + NCTX
    assert D == P and K1 == NF * D + NCOL and TILES % 2 == 0 and H1 == 512

    GF = 4
    GROUPS = [list(range(f, min(f + GF, NF))) for f in range(0, NF, GF)]
    NG = len(GROUPS)
    assert NG == 7
    ON_DVE = 3
    COL_CHUNKS = [(c, min(P, NCOL - c)) for c in range(0, NCOL, P)]
    FULL = NCOL // P
    W1_CHUNKS = NF + len(COL_CHUNKS)
    K2 = H1 // P
    PER = H1 // H2
    W_CHUNKS = W1_CHUNKS + K2 // PER
    STAGES = 6

    Q = 32
    R = NF - 1
    HALF = Q // 2

    ctx = ExitStack()
    with ctx:
        def sb(name, shape, dt=fp32):
            return ctx.enter_context(nc.sbuf_tensor(name, shape, dt))

        def ps(name, shape):
            return ctx.enter_context(nc.psum_tensor(name, shape, fp32))

        def sem(name):
            return ctx.enter_context(nc.semaphore(name))

        w_hi = sb("w_hi", [P, W_CHUNKS, H1], fp32r)
        w_lo = sb("w_lo", [P, W_CHUNKS, H1], fp32r)
        emb = sb("emb", [P, NF * D])
        emb_t = sb("emb_t", [P, 2, P * NF])
        emb_hi = sb("emb_hi", [P, 2, GF * P], fp32r)
        emb_lo = sb("emb_lo", [P, 2, GF * P], fp32r)
        idx = sb("idx", [P, 2, NF], i32)
        ident = sb("ident", [P, P])
        gram = sb("gram", [P, R, Q])
        cols = sb("cols", [P, 2, NCOL])
        cols_hi = sb("cols_hi", [P, len(COL_CHUNKS) * P], fp32r)
        cols_lo = sb("cols_lo", [P, len(COL_CHUNKS) * P], fp32r)
        h1 = sb("h1", [P, H1])
        h1_t = sb("h1_t", [P, H1])
        h1_hi = sb("h1_hi", [P, H1], fp32r)
        h1_lo = sb("h1_lo", [P, H1], fp32r)
        h2 = sb("h2", [P, H2])
        h2_w = sb("h2_w", [P, H2])
        y = sb("y", [P, TILES])
        b1_rows = sb("b1_rows", [P, H1])
        b2_rows = sb("b2_rows", [P, H2])
        w3_rows = sb("w3_rows", [P, H2])
        stage = emb_t[:, 1, 0:STAGES * H1].rearrange("p (s n) -> p s n", s=STAGES)

        ps_t = ps("ps_t", [P, 2, GF * P])
        ps_acc = ps("ps_acc", [P, 2, H1])
        ps_gram = ps("ps_gram", [P, 2, 512])
        ps_late = ps("ps_late", [P, 512])
        ps_h2 = ps("ps_h2", [P, 512])

        s_ids = [sem(f"s_ids{p}") for p in range(2)]
        s_ctx = [sem(f"s_ctx{p}") for p in range(2)]
        s_const = sem("s_const")
        s_w_raw = [sem(f"s_w_raw{s}") for s in range(STAGES)]
        s_gather = [sem(f"s_gather{g}") for g in range(NG)]
        s_started = sem("s_started")
        s_zero = sem("s_zero")
        s_ident = sem("s_ident")
        s_gram_clear = sem("s_gram_clear")
        s_w_hi = sem("s_w_hi")
        s_w_lo = sem("s_w_lo")
        s_pe_t = sem("s_pe_t")
        s_dve_t = sem("s_dve_t")
        s_emb_x = sem("s_emb_x")
        s_emb_lo = sem("s_emb_lo")
        s_emb_mm = sem("s_emb_mm")
        s_gram = sem("s_gram")
        s_gram_out = sem("s_gram_out")
        s_cols = sem("s_cols")
        s_cols_t = sem("s_cols_t")
        s_cols_hi = sem("s_cols_hi")
        s_cols_lo = sem("s_cols_lo")
        s_acc = sem("s_acc")
        s_h1 = sem("s_h1")
        s_h1_t = sem("s_h1_t")
        s_end_h1 = sem("s_end_h1")
        s_end_t = sem("s_end_t")
        s_end_hi = sem("s_end_hi")
        s_end_lo = sem("s_end_lo")
        s_h1_hi = sem("s_h1_hi")
        s_h1_lo = sem("s_h1_lo")
        s_l2 = sem("s_l2")
        s_h2 = sem("s_h2")
        s_y = sem("s_y")
        s_stored = sem("s_stored")

        LAST = (TILES - 1, TILES // 2 - 1, 1)

        def over_tiles(eng, tile):
            tile((0, 0, 0), None)
            tile((1, 0, 1), (0, 0, 0))
            with eng.Fori(1, TILES // 2) as i:
                tile((2 * i, i, 0), (2 * i - 1, i - 1, 1))
                tile((2 * i + 1, i, 1), (2 * i, i, 0))

        def is_first(t, n=1):
            return isinstance(t, int) and t < n

        def turned_group(p, g):
            features = emb_t[:, p, :].rearrange("p (b f) -> p f b", f=NF)
            return features[:, GROUPS[g][0]:GROUPS[g][-1] + 1, :]

        def by_feature(group):
            return group.rearrange("p (f b) -> p f b", b=P)

        def is_last(t):
            return isinstance(t, int) and t == TILES - 1

        def end_bank(k):
            return [ps_t[:, 0, 0:P], ps_t[:, 1, 0:P], ps_gram[:, 0, 0:P], ps_gram[:, 1, 0:P]][k]

        def transposed(t, g):
            if is_first(t):
                return s_pe_t, g + 1
            if g == ON_DVE:
                return s_dve_t, t
            return s_pe_t, (NG - 1) * t + 2 + g - (g > ON_DVE)

        block = ctx.enter_context(nc.Block())

        @block.sync
        def _(sp):
            def load_ids(t, p):
                sp.dma_start(idx[:, p, :], ids[bass.ds(t * P, P), :]).then_inc(s_ids[p], 16)

            def load_ctx(t, p):
                sp.dma_start(cols[:, p, NPAIR:NCOL],
                             dense_ctx[bass.ds(t * P, P), :]).then_inc(s_ctx[p], 16)

            def load_weights(c):
                if c >= STAGES:
                    sp.wait_ge(s_w_lo, c - STAGES + 1)
                s = c % STAGES
                if c < W1_CHUNKS:
                    rows = min(P, K1 - c * P)
                    sp.dma_start(stage[0:rows, s, :],
                                 w_top1[c * P:c * P + rows, :]).then_inc(s_w_raw[s], 16)
                else:
                    k = (c - W1_CHUNKS) * PER
                    sp.dma_start(stage[:, s, :].rearrange("p (k n) -> p k n", k=PER),
                                 w_top2[k * P:(k + PER) * P, :].rearrange("(k p) n -> p k n", p=P)
                                 ).then_inc(s_w_raw[s], 16)

            def store(t):
                sp.wait_ge(s_y, t + 1)
                sp.dma_start(out[bass.ds(t * P, P), :], y[:, bass.ds(t, 1)]).then_inc(s_stored, 16)

            load_ids(0, 0)
            load_weights(0)
            load_ids(1, 1)
            for c in range(1, W_CHUNKS):
                load_weights(c)

            def load_next(t, p):
                sp.wait_ge(s_emb_x, NG * t)
                load_ids(t + 1, 1 - p)
                sp.wait_ge(s_cols_t, t)
                load_ctx(t + 1, 1 - p)

            load_next(1, 1)
            with sp.Fori(1, TILES // 2 - 1) as i:
                load_next(2 * i, 0)
                store(2 * i - 2)
                load_next(2 * i + 1, 1)
                store(2 * i - 1)
            load_next(TILES - 2, 0)
            for t in range(TILES - 4, TILES):
                store(t)
            sp.wait_ge(s_stored, 16 * TILES)

        @block.gpsimd
        def _(pool):
            pool.memset(ident[:, :], 0.0).then_inc(s_zero, 1)
            pool.wait_ge(s_zero, 1)
            pool.affine_select(out=ident[:, :], in_=ident[:, :], compare_op=ALU.not_equal, fill=1.0,
                               base=0, pattern=[[-1, P]], channel_multiplier=1).then_inc(s_ident, 1)

            def tile(now, before):
                t, u, p = now
                pool.wait_ge(s_ids[p], 16 * u + 16)
                for g in range(NG):
                    if not is_first(t):
                        pool.wait_ge(*transposed(before[0], g))
                    pool.sem_inc(s_started, 1)
                    for f in GROUPS[g]:
                        pool.indirect_dma_start(
                            out=emb[:, f * D:(f + 1) * D], out_offset=None, in_=tables[f],
                            in_offset=bass.IndirectOffsetOnAxis(ap=idx[:, p, f:f + 1], axis=0)
                        ).then_inc(s_gather[g], 16)

            over_tiles(pool, tile)

        @block.tensor
        def _(pe):
            def transpose_group(t, p, g):
                slot = (p + g) % 2
                group = GROUPS[g]
                pe.wait_ge(s_gather[g], (t + 1) * (16 * len(group)))
                if not (is_first(t) and g < 2):
                    pe.wait_ge(s_emb_lo, NG * t + g - 1)
                for n, f in enumerate(group):
                    last = pe.transpose(ps_t[:, slot, n * P:(n + 1) * P],
                                        emb[:, f * D:(f + 1) * D], ident[:, :])
                last.then_inc(s_pe_t, 1)

            def split_product(acc, x_hi, x_lo, c, lo, hi, start, stop):
                rows = x_hi.shape[0]
                pe.matmul(acc, x_hi, w_hi[0:rows, c, lo:hi], start=start, stop=False)
                pe.matmul(acc, x_hi, w_lo[0:rows, c, lo:hi], start=False, stop=False)
                return pe.matmul(acc, x_lo, w_hi[0:rows, c, lo:hi], start=False, stop=stop)

            def multiply_group(t, p, g):
                slot = (p + g) % 2
                if g == 0 and not is_first(t, 2):
                    pe.wait_ge(s_h1, t - 1)
                pe.wait_ge(s_emb_lo, NG * t + g + 1)
                if is_first(t):
                    pe.wait_ge(s_w_lo, GROUPS[g][-1] + 1)
                for n, f in enumerate(GROUPS[g]):
                    last = split_product(ps_acc[:, p, :], emb_hi[:, slot, n * P:(n + 1) * P],
                                         emb_lo[:, slot, n * P:(n + 1) * P], f, 0, H1,
                                         start=(f == 0), stop=False)
                last.then_inc(s_emb_mm, 1)

            def gram_matrices(t, p, half):
                if half == 0:
                    pe.wait_ge(s_emb_x, NG * t + NG)
                    if is_first(t):
                        pe.wait_ge(s_gram_clear, 1)
                    else:
                        pe.wait_ge(s_gram_out, t)
                for q in range(half * HALF, (half + 1) * HALF):
                    for j in range(P // Q):
                        sample = emb_t[:, p, (j * Q + q) * NF:(j * Q + q + 1) * NF]
                        last = pe.matmul(
                            ps_gram[j * Q:j * Q + R, q // HALF, (q % HALF) * R:(q % HALF + 1) * R],
                            sample[:, 0:R], sample[:, 1:NF], start=True, stop=True,
                            tile_position=(0, j * Q))
                if half == 1:
                    last.then_inc(s_gram, 1)

            def transpose_columns(t, u, p):
                pe.wait_ge(s_cols, t + 1)
                pe.wait_ge(s_ctx[p], 16 * u + 16)
                for n, (c, k) in enumerate(COL_CHUNKS):
                    last = pe.transpose(ps_late[0:k, n * P:(n + 1) * P], cols[:, p, c:c + k],
                                        ident[:, :])
                last.then_inc(s_cols_t, 1)

            def multiply_columns(t, p):
                pe.wait_ge(s_cols_hi, t + 1)
                pe.wait_ge(s_cols_lo, t + 1)
                for n, (c, k) in enumerate(COL_CHUNKS):
                    last = split_product(ps_acc[:, p, :], cols_hi[0:k, n * P:(n + 1) * P],
                                         cols_lo[0:k, n * P:(n + 1) * P], NF + n, 0, H1,
                                         start=False, stop=(n == len(COL_CHUNKS) - 1))
                last.then_inc(s_acc, 1)

            def layer_2(t):
                pe.wait_ge(s_h2, t + 1)
                if is_last(t):
                    for k in range(K2):
                        pe.wait_ge(s_end_h1, k + 1)
                        pe.transpose(end_bank(k), h1[:, k * P:(k + 1) * P],
                                     ident[:, :]).then_inc(s_end_t, 1)
                else:
                    pe.wait_ge(s_h1_hi, t + 1)
                    pe.wait_ge(s_h1_lo, t + 1)
                for k in range(K2):
                    if is_last(t):
                        pe.wait_ge(s_end_lo, k + 1)
                    last = split_product(ps_h2[:, 0:H2], h1_hi[:, k * P:(k + 1) * P],
                                         h1_lo[:, k * P:(k + 1) * P], W1_CHUNKS + k // PER,
                                         (k % PER) * H2, (k % PER + 1) * H2,
                                         start=(k == 0), stop=(k == K2 - 1))
                last.then_inc(s_l2, 1)

            def finish_tile(now):
                t, u, p = now
                gram_matrices(t, p, 1)
                multiply_group(t, p, NG - 1)
                if is_last(t):
                    transpose_columns(*LAST)
                if not is_first(t):
                    layer_2(t - 1)

            def tile(now, before):
                t, u, p = now
                if before is None:
                    transpose_group(t, p, 0)
                    for g in range(NG - 1):
                        transpose_group(t, p, g + 1)
                        multiply_group(t, p, g)
                    gram_matrices(t, p, 0)
                    pe.wait_ge(s_w_lo, W_CHUNKS)
                    return
                transpose_group(t, p, 0)
                finish_tile(before)
                transpose_group(t, p, 1)
                multiply_group(t, p, 0)
                transpose_group(t, p, 2)
                multiply_group(t, p, 1)
                transpose_columns(*before)
                multiply_group(t, p, 2)
                multiply_columns(before[0], before[2])
                transpose_group(t, p, 4)
                multiply_group(t, p, 3)
                transpose_group(t, p, 5)
                multiply_group(t, p, 4)
                transpose_group(t, p, 6)
                multiply_group(t, p, 5)
                gram_matrices(t, p, 0)

            pe.wait_ge(s_ident, 1)
            over_tiles(pe, tile)
            finish_tile(LAST)
            multiply_columns(LAST[0], LAST[2])
            layer_2(LAST[0])

        @block.scalar
        def _(act):
            def split_weights(c):
                rows = min(P, K1 - c * P) if c < W1_CHUNKS else P
                act.wait_ge(s_w_raw[c % STAGES], 16 * (c // STAGES + 1))
                act.activation(w_hi[0:rows, c, :], stage[0:rows, c % STAGES, :],
                               ACT.Copy).then_inc(s_w_hi, 1)

            def copy_group(t, p, g):
                slot = (p + g) % 2
                n = len(GROUPS[g]) * P
                act.wait_ge(*transposed(t, g))
                if not (is_first(t) and g < 2):
                    act.wait_ge(s_emb_mm, NG * t + g - 1)
                if g == ON_DVE and not is_first(t):
                    act.activation(by_feature(emb_hi[:, slot, 0:n]), turned_group(p, g),
                                   ACT.Copy).then_inc(s_emb_x, 1)
                    return
                act.activation(emb_hi[:, slot, 0:n], ps_t[:, slot, 0:n], ACT.Copy)
                act.activation(turned_group(p, g), by_feature(ps_t[:, slot, 0:n]),
                               ACT.Copy).then_inc(s_emb_x, 1)

            def split_columns(t):
                act.wait_ge(s_cols_t, t + 1)
                if not is_first(t):
                    act.wait_ge(s_acc, t)
                act.activation(cols_hi[:, 0:FULL * P], ps_late[:, 0:FULL * P], ACT.Copy)
                k = NCOL - FULL * P
                act.activation(cols_hi[0:k, FULL * P:(FULL + 1) * P],
                               ps_late[0:k, FULL * P:(FULL + 1) * P],
                               ACT.Copy).then_inc(s_cols_hi, 1)

            def split_h1(t):
                act.wait_ge(s_h1_t, t + 1)
                if not is_first(t):
                    act.wait_ge(s_l2, t)
                act.activation(h1_hi[:, :], h1_t[:, :], ACT.Relu).then_inc(s_h1_hi, 1)

            act.dma_start(cols[:, 0, NPAIR:NCOL], dense_ctx[0:P, :]).then_inc(s_ctx[0], 16)
            act.dma_start(cols[:, 1, NPAIR:NCOL], dense_ctx[P:2 * P, :]).then_inc(s_ctx[1], 16)
            act.dma_start(b1_rows[:, :], b_top1.partition_broadcast(P)).then_inc(s_const, 16)
            act.dma_start(b2_rows[:, :], b_top2.partition_broadcast(P)).then_inc(s_const, 16)
            act.dma_start(w3_rows[:, :],
                          w_top3.rearrange("k o -> (k o)").partition_broadcast(P)
                          ).then_inc(s_const, 16)

            def tile(now, before):
                t, u, p = now
                if before is None:
                    for g, group in enumerate(GROUPS):
                        for c in group:
                            split_weights(c)
                        copy_group(t, p, g)
                    for c in range(NF, W_CHUNKS):
                        split_weights(c)
                    act.wait_ge(s_w_lo, W_CHUNKS)
                    return
                if not is_first(t, 2):
                    act.wait_ge(s_gram, t - 1)
                for g in range(NG):
                    copy_group(t, p, g)
                    if g == 2:
                        split_columns(before[0])
                split_h1(before[0])

            over_tiles(act, tile)
            split_columns(TILES - 1)
            act.wait_ge(s_l2, TILES - 1)
            for k in range(K2):
                act.wait_ge(s_end_t, k + 1)
                act.activation(h1_hi[:, k * P:(k + 1) * P], end_bank(k),
                               ACT.Relu).then_inc(s_end_hi, 1)

        @block.vector
        def _(dve):
            def split_weights(c):
                rows = min(P, K1 - c * P) if c < W1_CHUNKS else P
                dve.wait_ge(s_w_hi, c + 1)
                dve.tensor_tensor(w_lo[0:rows, c, :], stage[0:rows, c % STAGES, :],
                                  w_hi[0:rows, c, :].bitcast(fp32),
                                  ALU.subtract).then_inc(s_w_lo, 1)

            def split_group(t, p, g):
                slot = (p + g) % 2
                n = len(GROUPS[g]) * P
                dve.wait_ge(s_emb_x, NG * t + g + 1)
                x = by_feature(ps_t[:, slot, 0:n])
                if g == ON_DVE and not is_first(t):
                    x = turned_group(p, g)
                dve.tensor_tensor(by_feature(emb_lo[:, slot, 0:n]), x,
                                  by_feature(emb_hi[:, slot, 0:n].bitcast(fp32)),
                                  ALU.subtract).then_inc(s_emb_lo, 1)

            def turn_blocks(turned, rows, i):
                rows = rows.rearrange("p (k c) -> p k c", c=P)
                for j in range(P // Q):
                    last = dve.transpose(turned[j * Q:(j + 1) * Q, :, i * Q:(i + 1) * Q],
                                         rows[i * Q:(i + 1) * Q, :, j * Q:(j + 1) * Q])
                return last

            def transpose_group(t, p, i):
                group = GROUPS[ON_DVE]
                if i == 0:
                    dve.wait_ge(s_gather[ON_DVE], (t + 1) * (16 * len(group)))
                    if not is_first(t, 2):
                        dve.wait_ge(s_gram, t - 1)
                last = turn_blocks(turned_group(p, ON_DVE),
                                   emb[:, group[0] * D:(group[-1] + 1) * D], i)
                if i == P // Q - 1:
                    last.then_inc(s_dve_t, 1)

            def move_gram(t):
                dve.wait_ge(s_gram, t + 1)
                dve.transpose(gram[:, :, :].rearrange("p g f -> p (g f)"),
                              ps_gram[:, :, 0:HALF * R].rearrange("p h (q g) -> p g h q", g=R)
                              ).then_inc(s_gram_out, 1)

            def pack_pairs(t, p, f_from, f_to):
                if f_from == 0:
                    dve.wait_ge(s_gram_out, t + 1)
                    if not is_first(t):
                        dve.wait_ge(s_cols_t, t)
                for f in range(f_from, f_to):
                    c = f * NF - f * (f + 1) // 2
                    last = dve.tensor_copy(cols[:, p, c:c + R - f], gram[:, f:R, f])
                if f_to == R:
                    last.then_inc(s_cols, 1)

            def split_columns(t):
                dve.wait_ge(s_cols_hi, t + 1)
                dve.tensor_tensor(cols_lo[:, 0:FULL * P], ps_late[:, 0:FULL * P],
                                  cols_hi[:, 0:FULL * P].bitcast(fp32), ALU.subtract)
                k = NCOL - FULL * P
                last = slice(FULL * P, (FULL + 1) * P)
                dve.tensor_tensor(cols_lo[0:k, last], ps_late[0:k, last],
                                  cols_hi[0:k, last].bitcast(fp32),
                                  ALU.subtract).then_inc(s_cols_lo, 1)

            def bias_h1(t, p):
                dve.wait_ge(s_acc, t + 1)
                dve.tensor_tensor(h1[:, :], ps_acc[:, p, :], b1_rows[:, :],
                                  ALU.add).then_inc(s_h1, 1)

            def transpose_h1(t, i):
                if i == 0:
                    dve.wait_ge(s_h1, t + 1)
                last = turn_blocks(by_feature(h1_t[:, :]), h1[:, :], i)
                if i == P // Q - 1:
                    last.then_inc(s_h1_t, 1)

            def split_h1(t):
                dve.wait_ge(s_h1_hi, t + 1)
                dve.scalar_tensor_tensor(out=h1_lo[:, :], in0=h1_t[:, :], scalar=0.0,
                                         in1=h1_hi[:, :].bitcast(fp32), op0=ALU.max,
                                         op1=ALU.subtract).then_inc(s_h1_lo, 1)

            def layer_3(t):
                dve.wait_ge(s_l2, t + 1)
                dve.tensor_tensor(h2[:, :], ps_h2[:, 0:H2], b2_rows[:, :],
                                  ALU.add).then_inc(s_h2, 1)
                dve.wait_ge(s_h2, t + 2)
                dve.scalar_tensor_tensor(out=h2_w[:, :], in0=h2[:, :], scalar=0.0,
                                         in1=w3_rows[:, :], op0=ALU.max, op1=ALU.mult,
                                         accum_out=y[:, bass.ds(t, 1)]).then_inc(s_y, 1)

            def tile(now, before):
                t, u, p = now
                if before is None:
                    for g, group in enumerate(GROUPS):
                        for c in group:
                            split_weights(c)
                        split_group(t, p, g)
                    for c in range(NF, W_CHUNKS):
                        split_weights(c)
                    dve.wait_ge(s_const, 48)
                    return
                split_group(t, p, 0)
                move_gram(before[0])
                pack_pairs(before[0], before[2], 0, 12)
                split_group(t, p, 1)
                pack_pairs(before[0], before[2], 12, R)
                if not is_first(t, 2):
                    layer_3(t - 2)
                split_group(t, p, 2)
                transpose_group(t, p, 0)
                transpose_group(t, p, 1)
                split_columns(before[0])
                transpose_group(t, p, 2)
                transpose_group(t, p, 3)
                split_group(t, p, 3)
                bias_h1(before[0], before[2])
                transpose_h1(before[0], 0)
                split_group(t, p, 4)
                transpose_h1(before[0], 1)
                transpose_h1(before[0], 2)
                split_group(t, p, 5)
                transpose_h1(before[0], 3)
                split_group(t, p, 6)
                split_h1(before[0])

            dve.memset(ps_gram[:, :, :], 0.0).then_inc(s_gram_clear, 1)
            dve.sem_inc(s_h2, 1)
            over_tiles(dve, tile)
            t, u, p = LAST
            move_gram(t)
            pack_pairs(t, p, 0, R)
            split_columns(t)
            layer_3(t - 1)
            dve.wait_ge(s_acc, t + 1)
            for k in range(K2):
                chunk = slice(k * P, (k + 1) * P)
                dve.tensor_tensor(h1[:, chunk], ps_acc[:, p, chunk], b1_rows[:, chunk],
                                  ALU.add).then_inc(s_end_h1, 1)
            for k in range(K2):
                chunk = slice(k * P, (k + 1) * P)
                dve.wait_ge(s_end_hi, k + 1)
                dve.scalar_tensor_tensor(out=h1_lo[:, chunk], in0=end_bank(k), scalar=0.0,
                                         in1=h1_hi[:, chunk].bitcast(fp32), op0=ALU.max,
                                         op1=ALU.subtract).then_inc(s_end_lo, 1)
            layer_3(t)


N_TABLES = 27
_INS = (["dense_ctx", "ids"] + [f"tbl_{i}" for i in range(N_TABLES)]
        + ["W_top1", "b_top1", "W_top2", "b_top2", "W_top3"])


def kernel(**inputs):
    import numpy as np
    import concourse.bacc as bacc
    from concourse.bass_utils import run_bass_kernel_spmd

    nc = bacc.Bacc("TRN2", target_bir_lowering=False, num_devices=1)
    arrays, aps = {}, {}
    for name in _INS:
        a = np.ascontiguousarray(inputs[name])
        arrays[f"in_{name}"] = a
        aps[name] = nc.dram_tensor(f"in_{name}", a.shape, mybir.dt.from_np(a.dtype),
                                   kind="ExternalInput").ap()
    batch = inputs["ids"].shape[0]
    out = nc.dram_tensor("out", (batch, 1), mybir.dt.float32, kind="ExternalOutput").ap()
    dlrm_tower_kernel(nc, aps["dense_ctx"], aps["ids"], [aps[f"tbl_{i}"] for i in range(N_TABLES)],
                      aps["W_top1"], aps["b_top1"], aps["W_top2"], aps["b_top2"], aps["W_top3"], out)
    r = run_bass_kernel_spmd(nc, [arrays], core_ids=[0])
    return r.results[0]["out"]
```
